# Optimizing a Trainium2 kernel written in Bass

```python
import numpy as np
import jax
import jax.numpy as jnp

def _softmax(x, axis=-1):
    return jax.nn.softmax(x, axis=axis)

def _gelu(x):
    return jax.nn.gelu(x, approximate=True)

def _silu(x):
    return jax.nn.silu(x)

def _sigmoid(x):
    return jax.nn.sigmoid(x)

def _layernorm(x, axis=-1, eps=1e-05):
    m = jnp.mean(x, axis=axis, keepdims=True)
    v = jnp.var(x, axis=axis, keepdims=True)
    return (x - m) / jnp.sqrt(v + eps)

def _scatter_add(tgt, idx, src, axis=0):
    return tgt.at[idx].add(src)

def _segment_sum(src, seg, n):
    return jax.ops.segment_sum(src, seg, n)
kernel_name = 'mk_prb_d1_jaxref_r8_17422f'

def setup_inputs(seed: int=0):
    np.random.seed(seed)
    _w = jnp.asarray

    def _L0_attn_setup():
        import jax, jax.numpy as jnp
        import numpy as np
        DECAY = 0.99
        T_BLK = 128

        def _decay_mats(N_blk, dtype):
            i = jnp.arange(T_BLK, dtype=jnp.float32)[:, None]
            j = jnp.arange(T_BLK, dtype=jnp.float32)[None, :]
            decays = jnp.tril(jnp.asarray(DECAY, jnp.float32) ** (i - j)).astype(dtype)
            bi = jnp.arange(N_blk, dtype=jnp.float32)[:, None]
            bj = jnp.arange(N_blk, dtype=jnp.float32)[None, :]
            block_decay = DECAY ** T_BLK
            block_decays = jnp.tril(DECAY * jnp.asarray(block_decay, jnp.float32) ** (bi - bj)).astype(dtype)
            return (decays, block_decays)
        key = jax.random.key(seed)
        ks = jax.random.split(key, 8)
        B, T, E = (4, 512, 128)
        Dk, Dv = (128, 128)
        s = 0.02
        return {'x': jax.random.normal(ks[0], (B, T, E), jnp.float32), 'Wv': jax.random.normal(ks[1], (E, Dv), jnp.float32) * s, 'Wk': jax.random.normal(ks[2], (E, Dk), jnp.float32) * s, 'bk': jax.random.normal(ks[3], (Dk,), jnp.float32) * s, 'Wq': jax.random.normal(ks[4], (E, Dk), jnp.float32) * s, 'bq': jax.random.normal(ks[5], (Dk,), jnp.float32) * s, 'Wo': jax.random.normal(ks[6], (Dv, E), jnp.float32) * s}
    _L0_attn_in = _L0_attn_setup()

    def _L0_ffn_setup():
        import jax, jax.numpy as jnp
        import numpy as np
        DIM = 128
        HIDDEN = 384
        SCALE = 1.0 / 127.0

        def _dequant(w_int, dtype):
            return w_int.astype(dtype) * jnp.asarray(SCALE, dtype)
        key = jax.random.key(seed)
        k_x, k_g, k_u, k_d = jax.random.split(key, 4)
        x = jax.random.normal(k_x, (4, 256, DIM), dtype=jnp.float32)
        w_gate = jax.random.randint(k_g, (HIDDEN, DIM), -127, 128, dtype=jnp.int32)
        w_up = jax.random.randint(k_u, (HIDDEN, DIM), -127, 128, dtype=jnp.int32)
        w_down = jax.random.randint(k_d, (DIM, HIDDEN), -127, 128, dtype=jnp.int32)
        return {'x': x, 'w_gate': w_gate, 'w_up': w_up, 'w_down': w_down}
    _L0_ffn_in = _L0_ffn_setup()
    _d = {'L0_attn_x': _L0_attn_in['x'], 'L0_attn_Wv': _L0_attn_in['Wv'], 'L0_attn_Wk': _L0_attn_in['Wk'], 'L0_attn_bk': _L0_attn_in['bk'], 'L0_attn_Wq': _L0_attn_in['Wq'], 'L0_attn_bq': _L0_attn_in['bq'], 'L0_attn_Wo': _L0_attn_in['Wo'], 'L0_ffn_w_gate': _L0_ffn_in['w_gate'], 'L0_ffn_w_up': _L0_ffn_in['w_up'], 'L0_ffn_w_down': _L0_ffn_in['w_down']}
    _x0 = _d['L0_attn_x']
    _d['L0_attn_x'] = jax.random.normal(jax.random.fold_in(jax.random.key(seed), 1), (8, 512, 128), dtype=_x0.dtype)
    del _x0
    return _d

def reference(L0_attn_x, L0_attn_Wv, L0_attn_Wk, L0_attn_bk, L0_attn_Wq, L0_attn_bq, L0_attn_Wo, L0_ffn_w_gate, L0_ffn_w_up, L0_ffn_w_down):

    def _L0_attn_ref(x, Wv, Wk, bk, Wq, bq, Wo):
        import jax, jax.numpy as jnp
        import numpy as np
        DECAY = 0.99
        T_BLK = 128

        def _decay_mats(N_blk, dtype):
            i = jnp.arange(T_BLK, dtype=jnp.float32)[:, None]
            j = jnp.arange(T_BLK, dtype=jnp.float32)[None, :]
            decays = jnp.tril(jnp.asarray(DECAY, jnp.float32) ** (i - j)).astype(dtype)
            bi = jnp.arange(N_blk, dtype=jnp.float32)[:, None]
            bj = jnp.arange(N_blk, dtype=jnp.float32)[None, :]
            block_decay = DECAY ** T_BLK
            block_decays = jnp.tril(DECAY * jnp.asarray(block_decay, jnp.float32) ** (bi - bj)).astype(dtype)
            return (decays, block_decays)
        B, T, E = x.shape
        N_blk = T // T_BLK
        decays, block_decays = _decay_mats(N_blk, x.dtype)
        v = x @ Wv * (1.0 - DECAY)
        k = jax.nn.sigmoid(x @ Wk + bk)
        q = jax.nn.sigmoid(x @ Wq + bq)
        Dv, Dk = (v.shape[-1], k.shape[-1])
        v = v.reshape(B, N_blk, T_BLK, Dv)
        k = k.reshape(B, N_blk, T_BLK, Dk)
        q = q.reshape(B, N_blk, T_BLK, Dk)
        a = jnp.einsum('bntd,bnsd->bnts', q, k) * decays
        y = jnp.einsum('bnts,bnsv->bntv', a, v)
        kv_blk = jnp.einsum('bntd,bntv->bndv', k, v * decays[T_BLK - 1, :, None])
        kv2 = jnp.concatenate([jnp.zeros_like(kv_blk[:, :1]), kv_blk[:, :-1]], axis=1)
        kv = jnp.einsum('nm,bmdv->bndv', block_decays, kv2)
        y2 = jnp.einsum('bntd,bndv->bntv', q, kv) * decays[:, :1]
        y = (y + y2).reshape(B, T, Dv)
        return y @ Wo

    def _L0_ffn_ref(x, w_gate, w_up, w_down):
        import jax, jax.numpy as jnp
        import numpy as np
        DIM = 128
        HIDDEN = 384
        SCALE = 1.0 / 127.0

        def _dequant(w_int, dtype):
            return w_int.astype(dtype) * jnp.asarray(SCALE, dtype)
        wg = _dequant(w_gate, x.dtype)
        wu = _dequant(w_up, x.dtype)
        wd = _dequant(w_down, x.dtype)
        gate = jnp.einsum('bsd,hd->bsh', x, wg)
        up = jnp.einsum('bsd,hd->bsh', x, wu)
        h = jax.nn.silu(gate) * up
        return jnp.einsum('bsh,dh->bsd', h, wd)
    x = L0_attn_x
    xn = _layernorm(x, axis=-1)
    x = x + _L0_attn_ref(xn, L0_attn_Wv, L0_attn_Wk, L0_attn_bk, L0_attn_Wq, L0_attn_bq, L0_attn_Wo) + _L0_ffn_ref(xn, L0_ffn_w_gate, L0_ffn_w_up, L0_ffn_w_down)
    return x

_drawn_inputs = setup_inputs


def setup_inputs(seed=0):
    import zlib

    import numpy as np

    out = dict(_drawn_inputs(seed))
    spreads = {}
    factors = {'L0_attn_Wv': 22.209,
     'L0_attn_Wk': 64.0,
     'L0_attn_bk': 64.0,
     'L0_attn_Wq': 64.0,
     'L0_attn_bq': 64.0,
     'L0_attn_Wo': 22.449}
    for name, (base, spread) in spreads.items():
        noise = np.random.default_rng([zlib.crc32(name.encode()), seed]).standard_normal(out[name].shape)
        drawn = base * np.exp(spread * noise) if base else spread * noise
        out[name] = jnp.asarray(drawn.astype(out[name].dtype))
    for name, factor in factors.items():
        out[name] = (out[name] * factor).astype(out[name].dtype)
    return out
```

```python
from contextlib import ExitStack

import numpy as np

import concourse.bass as bass
from concourse import mybir

F32 = mybir.dt.float32
F32R = mybir.dt.float32r
I32 = mybir.dt.int32
ALU = mybir.AluOpType
ACT = mybir.ActivationFunctionType

P = 128
EPS = 1e-5
DECAY = 0.99
SCALE = 1.0 / 127.0


def build(nc, x, wv, wk, bk, wq, bq, wo, w_gate, w_up, w_down, causal_decay, query_decay, value_decay, out):
    B, T, E = x.shape
    HID = w_gate.shape[0]
    NB = T // P
    NH = HID // P
    LB = NB - 1
    assert E == P and T == 512 and wv.shape == (E, P) and wo.shape == (P, E)

    with ExitStack() as ctx:
        def sb(name, shape, dt=F32):
            return ctx.enter_context(nc.sbuf_tensor(name, shape, dt))

        def psum(name):
            return ctx.enter_context(nc.psum_tensor(name, [P, T], F32))

        def sem(name):
            return ctx.enter_context(nc.semaphore(name))

        identity = sb("identity", [P, P])
        wq_f = sb("wq_f", [P, P])
        wk_f = sb("wk_f", [P, P])
        wv_f = sb("wv_f", [P, P])
        wo_f = sb("wo_f", [P, P])
        wvT = sb("wvT", [P, P])
        wvo = sb("wvo", [P, P])
        bq_c = sb("bq_c", [P, 1])
        bk_c = sb("bk_c", [P, 1])
        ffn_int = sb("ffn_int", [P, 3, HID], I32)
        ffn_f = sb("ffn_f", [P, 3, HID])
        qk_hi = sb("qk_hi", [P, 2, P], F32R)
        qk_lo = sb("qk_lo", [P, 2, P], F32R)
        ffn_hi = sb("ffn_hi", [P, 3, NH, P], F32R)
        ffn_lo = sb("ffn_lo", [P, 3, NH, P], F32R)
        mask = sb("mask", [P, NB, P])
        q_dec = sb("q_dec", [P, LB * P])
        v_dec = sb("v_dec", [P, NB])
        minus_half = sb("minus_half", [P, NB])
        eps = sb("eps", [P, NB])

        x_all = sb("x_all", [P, B * NB, P])
        stats = sb("stats", [P, NB, 6])
        mean_var = sb("mean_var", [P, NB, 2])
        var_eps = sb("var_eps", [P, NB])
        rstd = sb("rstd", [P, NB])
        xn = sb("xn", [P, NB, P])
        xT = sb("xT", [P, T])
        xT_hi = sb("xT_hi", [P, T], F32R)
        xT_lo = sb("xT_lo", [P, T], F32R)
        qT = sb("qT", [P, T])
        kT = sb("kT", [P, T])
        q_state = sb("q_state", [P, LB * P])
        k_tok = sb("k_tok", [P, LB, P])
        v_tok = sb("v_tok", [P, NB, P])
        att = sb("att", [P, NB, P])
        state = sb("state", [P, LB, P])
        sig_g = sb("sig_g", [P, NH, T])
        silu_g = sb("silu_g", [P, NH, T])
        h = sb("h", [P, NH, T])
        h_hi = sb("h_hi", [P, NH, T], F32R)
        h_lo = sb("h_lo", [P, NH, T], F32R)
        oT = sb("oT", [P, T])
        y_out = sb("y_out", [P, NB, P])

        ps_t = psum("ps_t")
        ps_q = psum("ps_q")
        ps_k = psum("ps_k")
        ps_v = psum("ps_v")
        ps_g = psum("ps_g")
        ps_u = psum("ps_u")
        ps_a = psum("ps_a")
        ps_o = psum("ps_o")
        gate_bank = [ps_g, ps_q, ps_g]
        up_bank = [ps_u, ps_k, ps_u]

        attn_w_loaded = sem("attn_w_loaded")
        qk_w_loaded = sem("qk_w_loaded")
        ffn_w_loaded = [sem(f"ffn_w{i}_loaded") for i in range(3)]
        decay_loaded = sem("decay_loaded")
        blank_ready = sem("blank_ready")
        identity_ready = sem("identity_ready")
        norm_consts_ready = sem("norm_consts_ready")
        wvT_psum_ready = sem("wvT_psum_ready")
        wvT_ready = sem("wvT_ready")
        wvo_psum_ready = sem("wvo_psum_ready")
        wvo_ready = sem("wvo_ready")
        qk_hi_ready = sem("qk_hi_ready")
        qk_lo_ready = sem("qk_lo_ready")
        ffn_f_ready = sem("ffn_f_ready")
        ffn_psum_ready = sem("ffn_psum_ready")
        ffn_hi_ready = sem("ffn_hi_ready")
        ffn_lo_ready = sem("ffn_lo_ready")
        x_loaded = sem("x_loaded")
        stats_ready = sem("stats_ready")
        mean_var_ready = sem("mean_var_ready")
        var_eps_ready = sem("var_eps_ready")
        rstd_ready = sem("rstd_ready")
        xn_ready = sem("xn_ready")
        xT_psum_ready = sem("xT_psum_ready")
        xT_hi_ready = sem("xT_hi_ready")
        xT_lo_ready = sem("xT_lo_ready")
        xT_ready = sem("xT_ready")
        q_psum_ready = sem("q_psum_ready")
        k_psum_ready = sem("k_psum_ready")
        q_ready = sem("q_ready")
        k_ready = sem("k_ready")
        q_state_ready = sem("q_state_ready")
        v_psum_ready = sem("v_psum_ready")
        v_ready = sem("v_ready")
        att_psum_ready = sem("att_psum_ready")
        att_ready = sem("att_ready")
        k_tok_psum_ready = sem("k_tok_psum_ready")
        k_tok_ready = sem("k_tok_ready")
        kv_psum_ready = sem("kv_psum_ready")
        state_ready = sem("state_ready")
        gate_psum_ready = sem("gate_psum_ready")
        up_psum_ready = sem("up_psum_ready")
        sig_g_ready = sem("sig_g_ready")
        silu_ready = sem("silu_ready")
        h_ready = sem("h_ready")
        h_hi_ready = sem("h_hi_ready")
        h_lo_pool_ready = sem("h_lo_pool_ready")
        h_lo_dve_ready = sem("h_lo_dve_ready")
        oT_psum_ready = sem("oT_psum_ready")
        oT_ready = sem("oT_ready")
        out_psum_ready = sem("out_psum_ready")
        y_ready = sem("y_ready")
        y_stored = sem("y_stored")

        x_blocks = x.rearrange("b (n p) e -> b p n e", p=P)
        out_blocks = out.rearrange("b (n p) e -> b p n e", p=P)

        block = ctx.enter_context(nc.Block())

        @block.sync
        def _(sp):
            def load_x(b):
                sp.dma_start(x_all[:, bass.ds(b * NB, NB), :], x_blocks[b]).then_inc(x_loaded, 16)

            def store_y(b):
                sp.wait_ge(y_ready, b + 1)
                sp.dma_start(out_blocks[b], y_out[:, :, :]).then_inc(y_stored, 16)

            load_x(0)
            sp.dma_start(ffn_int[:, 0, :].rearrange("p (c e) -> p c e", e=E),
                         w_gate.rearrange("(c p) e -> p c e", p=P)).then_inc(ffn_w_loaded[0], 16)
            sp.dma_start(ffn_int[:, 1, :].rearrange("p (c e) -> p c e", e=E),
                         w_up.rearrange("(c p) e -> p c e", p=P)).then_inc(ffn_w_loaded[1], 16)
            sp.dma_start(ffn_int[:, 2, :], w_down).then_inc(ffn_w_loaded[2], 16)
            with sp.Fori(1, B) as b:
                sp.wait_ge(x_loaded, b * 16)
                load_x(b)
            with sp.Fori(0, B) as b:
                store_y(b)
            sp.wait_ge(y_stored, 16 * B)

        @block.gpsimd
        def _(pool):
            nc.gpsimd.memset(identity[:], 0.0).then_inc(blank_ready, 1)
            nc.gpsimd.memset(eps[:], EPS)
            nc.gpsimd.memset(minus_half[:], -0.5).then_inc(norm_consts_ready, 1)
            pool.wait_ge(blank_ready, 1)
            nc.gpsimd.affine_select(out=identity[:], in_=identity[:], compare_op=ALU.not_equal, fill=1.0,
                                    base=0, pattern=[[-1, P]], channel_multiplier=1).then_inc(identity_ready, 1)

            def norm(b):
                pool.wait_ge(mean_var_ready, b + 1)
                nc.gpsimd.tensor_tensor(var_eps[:], mean_var[:, :, 1], eps[:], ALU.add).then_inc(var_eps_ready, 1)
                pool.wait_ge(var_eps_ready, b + 1)
                nc.gpsimd.tensor_tensor(rstd[:], var_eps[:], minus_half[:], ALU.pow).then_inc(rstd_ready, 1)

            def whole_xT(b):
                pool.wait_ge(xT_lo_ready, b + 1)
                nc.gpsimd.tensor_tensor(xT[:], xT_hi[:].bitcast(F32), xT_lo[:].bitcast(F32), ALU.add).then_inc(xT_ready, 1)

            def sequence(b, last=False):
                if not last:
                    norm(b + 1)
                pool.wait_ge(q_ready, b + 1)
                nc.gpsimd.tensor_tensor(q_state[:], qT[:, P:T], q_dec[:], ALU.mult).then_inc(q_state_ready, 1)
                for c in range(NH - 1):
                    pool.wait_ge(h_hi_ready, b * NH + c + 1)
                    nc.gpsimd.tensor_tensor(h_lo[:, c], h[:, c], h_hi[:, c].bitcast(F32),
                                            ALU.subtract).then_inc(h_lo_pool_ready, 1)
                if not last:
                    whole_xT(b + 1)

            pool.wait_ge(norm_consts_ready, 1)
            norm(0)
            whole_xT(0)
            pool.wait_ge(decay_loaded, 48)
            sequence(0)
            with pool.Fori(1, B - 1) as b:
                sequence(b)
            sequence(B - 1, last=True)

        @block.scalar
        def _(act):
            act.dma_start(wv_f[:], wv).then_inc(attn_w_loaded, 16)
            act.dma_start(wo_f[:], wo).then_inc(attn_w_loaded, 16)
            act.dma_start(wq_f[:], wq).then_inc(qk_w_loaded, 16)
            act.dma_start(wk_f[:], wk).then_inc(qk_w_loaded, 16)
            act.dma_start(bq_c[:], bq.rearrange("(p o) -> p o", o=1)).then_inc(qk_w_loaded, 16)
            act.dma_start(bk_c[:], bk.rearrange("(p o) -> p o", o=1)).then_inc(qk_w_loaded, 16)
            act.dma_start(mask[:], causal_decay).then_inc(decay_loaded, 16)
            act.dma_start(q_dec[:], query_decay).then_inc(decay_loaded, 16)
            act.dma_start(v_dec[:], value_decay).then_inc(decay_loaded, 16)

            def copy_xT(b):
                act.wait_ge(xT_psum_ready, b + 1)
                nc.scalar.copy(xT_hi[:], ps_t[:]).then_inc(xT_hi_ready, 1)

            def sigmoid_gate(b, c):
                act.wait_ge(gate_psum_ready, b * NH + c + 1)
                nc.scalar.activation(sig_g[:, c], gate_bank[c][:], ACT.Sigmoid, scale=SCALE).then_inc(sig_g_ready, 1)

            def round_h(b, c):
                act.wait_ge(h_ready, b * NH + c + 1)
                nc.scalar.copy(h_hi[:, c], h[:, c]).then_inc(h_hi_ready, 1)

            def copy_oT(b):
                act.wait_ge(oT_psum_ready, b + 1)
                nc.scalar.copy(oT[:], ps_o[:]).then_inc(oT_ready, 1)

            def sequence(b, last=False):
                act.wait_ge(q_psum_ready, b + 1)
                nc.scalar.activation(qT[:], ps_q[:], ACT.Sigmoid, bias=bq_c[:]).then_inc(q_ready, 1)
                act.wait_ge(k_psum_ready, b + 1)
                nc.scalar.activation(kT[:], ps_k[:], ACT.Sigmoid, bias=bk_c[:]).then_inc(k_ready, 1)
                sigmoid_gate(b, 0)
                sigmoid_gate(b, 1)
                round_h(b, 0)
                act.wait_ge(k_tok_psum_ready, b + 1)
                nc.scalar.copy(k_tok[:].rearrange("p n e -> p (n e)"), ps_t[:, 0:LB * P]).then_inc(k_tok_ready, 1)
                sigmoid_gate(b, 2)
                round_h(b, 1)
                if not last:
                    copy_xT(b + 1)
                round_h(b, 2)
                copy_oT(b)

            act.wait_ge(wvT_psum_ready, 1)
            nc.scalar.copy(wvT[:], ps_v[:, 0:P]).then_inc(wvT_ready, 1)
            act.wait_ge(qk_w_loaded, 64)
            nc.scalar.copy(qk_hi[:, 0], wq_f[:]).then_inc(qk_hi_ready, 1)
            nc.scalar.copy(qk_hi[:, 1], wk_f[:]).then_inc(qk_hi_ready, 1)
            for m in range(3):
                act.wait_ge(ffn_w_loaded[m], 16)
                nc.scalar.copy(ffn_f[:, m], ffn_int[:, m]).then_inc(ffn_f_ready, 1)
            copy_xT(0)
            act.wait_ge(wvo_psum_ready, 1)
            nc.scalar.copy(wvo[:], ps_a[:, 0:P]).then_inc(wvo_ready, 1)
            for m, bank in enumerate((ps_g, ps_u, ps_o)):
                act.wait_ge(ffn_psum_ready, m + 1)
                nc.scalar.copy(ffn_hi[:, m].rearrange("p c e -> p (c e)"), bank[:, 0:HID]).then_inc(ffn_hi_ready, 1)
            sequence(0)
            with act.Fori(1, B - 1) as b:
                sequence(b)
            sequence(B - 1, last=True)

        @block.vector
        def _(dve):
            def norm_stats(b):
                dve.wait_ge(x_loaded, (b + 1) * 16)
                for n in range(NB):
                    nc.vector.bn_stats(stats[:, n], x_all[:, b * NB + n, :]).then_inc(stats_ready, 1)

            def norm_aggregate(b):
                for n in range(NB):
                    last = nc.vector.bn_aggr(mean_var[:, n], stats[:, n])
                last.then_inc(mean_var_ready, 1)

            def norm_apply(b):
                dve.wait_ge(mean_var_ready, b + 1)
                dve.wait_ge(rstd_ready, b + 1)
                for n in range(NB):
                    last = nc.vector.tensor_scalar(xn[:, n], x_all[:, b * NB + n, :], mean_var[:, n, 0:1], rstd[:, n:n + 1],
                                                   ALU.subtract, ALU.mult)
                last.then_inc(xn_ready, 1)

            def subtract_xT(b):
                dve.wait_ge(xT_hi_ready, b + 1)
                nc.vector.tensor_tensor(xT_lo[:], ps_t[:], xT_hi[:].bitcast(F32), ALU.subtract).then_inc(xT_lo_ready, 1)

            def residual(b):
                dve.wait_ge(out_psum_ready, b + 1)
                if not isinstance(b, int) or b > 0:
                    dve.wait_ge(y_stored, b * 16)
                nc.vector.tensor_tensor(y_out[:], ps_t[:].rearrange("p (n e) -> p n e", e=E),
                                        x_all[:, bass.ds(b * NB, NB), :], ALU.add).then_inc(y_ready, 1)

            def hidden(b, c, stats_of=None):
                if stats_of is not None:
                    dve.wait_ge(stats_ready, (stats_of + 1) * NB)
                dve.wait_ge(sig_g_ready, b * NH + c + 1)
                nc.vector.scalar_tensor_tensor(silu_g[:, c], gate_bank[c][:], SCALE, sig_g[:, c],
                                               ALU.mult, ALU.mult).then_inc(silu_ready, 1)
                dve.wait_ge(silu_ready, b * NH + c + 1)
                dve.wait_ge(up_psum_ready, b * NH + c + 1)
                nc.vector.scalar_tensor_tensor(h[:, c], up_bank[c][:], SCALE * SCALE, silu_g[:, c],
                                               ALU.mult, ALU.mult).then_inc(h_ready, 1)

            def sequence(b, first=False, last=False):
                if not first:
                    residual(b - 1)
                if not last:
                    norm_stats(b + 1)
                hidden(b, 0, stats_of=None if last else b + 1)
                if not last:
                    norm_aggregate(b + 1)
                dve.wait_ge(v_psum_ready, b + 1)
                nc.vector.tensor_tensor(v_tok[:], ps_v[:].rearrange("p (n e) -> p n e", e=E),
                                        v_dec[:].rearrange("p (n o) -> p n o", o=1).broadcast_to([P, NB, P]),
                                        ALU.mult).then_inc(v_ready, 1)
                dve.wait_ge(att_psum_ready, b + 1)
                nc.vector.tensor_tensor(att[:], ps_a[:].rearrange("p (n t) -> p n t", t=P), mask[:],
                                        ALU.mult).then_inc(att_ready, 1)
                hidden(b, 1)
                if not last:
                    norm_apply(b + 1)
                hidden(b, 2)
                dve.wait_ge(kv_psum_ready, b + 1)
                nc.vector.tensor_copy(state[:, 0], ps_v[:, 0:P]).then_inc(state_ready, 1)
                for n in range(1, LB):
                    dve.wait_ge(state_ready, b * LB + n)
                    nc.vector.tensor_tensor(state[:, n], ps_v[:, n * P:(n + 1) * P], state[:, n - 1],
                                            ALU.add).then_inc(state_ready, 1)
                if not last:
                    subtract_xT(b + 1)
                dve.wait_ge(h_hi_ready, (b + 1) * NH)
                nc.vector.tensor_tensor(h_lo[:, NH - 1], h[:, NH - 1], h_hi[:, NH - 1].bitcast(F32),
                                        ALU.subtract).then_inc(h_lo_dve_ready, 1)

            norm_stats(0)
            dve.wait_ge(stats_ready, NB)
            norm_aggregate(0)
            dve.wait_ge(qk_hi_ready, 1)
            nc.vector.tensor_tensor(qk_lo[:, 0], wq_f[:], qk_hi[:, 0].bitcast(F32), ALU.subtract).then_inc(qk_lo_ready, 1)
            dve.wait_ge(qk_hi_ready, 2)
            nc.vector.tensor_tensor(qk_lo[:, 1], wk_f[:], qk_hi[:, 1].bitcast(F32), ALU.subtract).then_inc(qk_lo_ready, 1)
            norm_apply(0)
            subtract_xT(0)
            for m, bank in enumerate((ps_g, ps_u, ps_o)):
                dve.wait_ge(ffn_hi_ready, m + 1)
                nc.vector.tensor_tensor(ffn_lo[:, m].rearrange("p c e -> p (c e)"), bank[:, 0:HID],
                                        ffn_hi[:, m].rearrange("p c e -> p (c e)").bitcast(F32),
                                        ALU.subtract).then_inc(ffn_lo_ready, 1)
            dve.wait_ge(decay_loaded, 48)
            sequence(0, first=True)
            with dve.Fori(1, B - 1) as b:
                sequence(b)
            sequence(B - 1, last=True)
            residual(B - 1)

        @block.tensor
        def _(pe):
            def split_product(bank, w_hi, w_lo, x_hi, x_lo, start=True, stop=True):
                nc.tensor.matmul(bank[:], w_hi, x_hi, start=start, stop=False)
                nc.tensor.matmul(bank[:], w_hi, x_lo, start=False, stop=False)
                return nc.tensor.matmul(bank[:], w_lo, x_hi, start=False, stop=stop)

            def transpose_xn(b):
                pe.wait_ge(xn_ready, b + 1)
                for n in range(NB):
                    last = nc.tensor.transpose(ps_t[:, n * P:(n + 1) * P], xn[:, n], identity[:])
                last.then_inc(xT_psum_ready, 1)

            def transpose_out(b):
                pe.wait_ge(oT_ready, b + 1)
                for n in range(NB):
                    last = nc.tensor.transpose(ps_t[:, n * P:(n + 1) * P], oT[:, n * P:(n + 1) * P], identity[:])
                last.then_inc(out_psum_ready, 1)

            def gate_up(b, c):
                split_product(gate_bank[c], ffn_hi[:, 0, c], ffn_lo[:, 0, c],
                              xT_hi[:], xT_lo[:]).then_inc(gate_psum_ready, 1)
                split_product(up_bank[c], ffn_hi[:, 1, c], ffn_lo[:, 1, c],
                              xT_hi[:], xT_lo[:]).then_inc(up_psum_ready, 1)

            def down(b, c, stop=False):
                if c < NH - 1:
                    pe.wait_ge(h_lo_pool_ready, b * (NH - 1) + c + 1)
                else:
                    pe.wait_ge(h_lo_dve_ready, b + 1)
                return split_product(ps_o, ffn_hi[:, 2, c], ffn_lo[:, 2, c], h_hi[:, c], h_lo[:, c],
                                     start=False, stop=stop)

            def sequence(b, first=False, last=False):
                pe.wait_ge(xT_hi_ready, b + 1)
                pe.wait_ge(xT_lo_ready, b + 1)
                split_product(ps_q, qk_hi[:, 0], qk_lo[:, 0], xT_hi[:], xT_lo[:]).then_inc(q_psum_ready, 1)
                split_product(ps_k, qk_hi[:, 1], qk_lo[:, 1], xT_hi[:], xT_lo[:]).then_inc(k_psum_ready, 1)
                if not first:
                    transpose_out(b - 1)
                gate_up(b, 0)
                pe.wait_ge(xT_ready, b + 1)
                for n in range(NB):
                    mm = nc.tensor.matmul(ps_v[:, n * P:(n + 1) * P], xT[:, n * P:(n + 1) * P], wvo[:], start=True, stop=True)
                mm.then_inc(v_psum_ready, 1)
                pe.wait_ge(q_ready, b + 1)
                pe.wait_ge(k_ready, b + 1)
                for n in range(NB):
                    mm = nc.tensor.matmul(ps_a[:, n * P:(n + 1) * P], kT[:, n * P:(n + 1) * P], qT[:, n * P:(n + 1) * P],
                                          start=True, stop=True)
                mm.then_inc(att_psum_ready, 1)
                gate_up(b, 1)
                if not first:
                    pe.wait_ge(y_ready, b)
                for n in range(LB):
                    mm = nc.tensor.transpose(ps_t[:, n * P:(n + 1) * P], kT[:, n * P:(n + 1) * P], identity[:])
                mm.then_inc(k_tok_psum_ready, 1)
                pe.wait_ge(h_ready, b * NH + 1)
                gate_up(b, 2)
                pe.wait_ge(k_tok_ready, b + 1)
                pe.wait_ge(v_ready, b + 1)
                for n in range(LB):
                    mm = nc.tensor.matmul(ps_v[:, n * P:(n + 1) * P], k_tok[:, n], v_tok[:, n], start=True, stop=True)
                mm.then_inc(kv_psum_ready, 1)
                if not last:
                    transpose_xn(b + 1)
                pe.wait_ge(att_ready, b + 1)
                for n in range(NB):
                    nc.tensor.matmul(ps_o[:, n * P:(n + 1) * P], v_tok[:, n], att[:, n], start=(n == 0), stop=False)
                for c in range(NH - 1):
                    down(b, c)
                pe.wait_ge(q_state_ready, b + 1)
                for n in range(LB):
                    pe.wait_ge(state_ready, b * LB + n + 1)
                    nc.tensor.matmul(ps_o[:, (n + 1) * P:(n + 2) * P], state[:, n], q_state[:, n * P:(n + 1) * P],
                                     start=False, stop=False)
                down(b, NH - 1, stop=True).then_inc(oT_psum_ready, 1)

            pe.wait_ge(identity_ready, 1)
            pe.wait_ge(attn_w_loaded, 32)
            nc.tensor.transpose(ps_v[:, 0:P], wv_f[:], identity[:]).then_inc(wvT_psum_ready, 1)
            pe.wait_ge(wvT_ready, 1)
            nc.tensor.matmul(ps_a[:, 0:P], wvT[:], wo_f[:], start=True, stop=True).then_inc(wvo_psum_ready, 1)
            transpose_xn(0)
            for m, bank in enumerate((ps_g, ps_u, ps_o)):
                pe.wait_ge(ffn_f_ready, m + 1)
                for c in range(NH):
                    mm = nc.tensor.transpose(bank[:, c * P:(c + 1) * P], ffn_f[:, m, c * P:(c + 1) * P], identity[:])
                mm.then_inc(ffn_psum_ready, 1)
            pe.wait_ge(wvo_ready, 1)
            pe.wait_ge(qk_lo_ready, 2)
            pe.wait_ge(ffn_lo_ready, 3)
            sequence(0, first=True)
            with pe.Fori(1, B - 1) as b:
                sequence(b)
            sequence(B - 1, last=True)
            transpose_out(B - 1)


_INS = {"x": "L0_attn_x", "wv": "L0_attn_Wv", "wk": "L0_attn_Wk", "bk": "L0_attn_bk", "wq": "L0_attn_Wq",
        "bq": "L0_attn_bq", "wo": "L0_attn_Wo", "w_gate": "L0_ffn_w_gate", "w_up": "L0_ffn_w_up", "w_down": "L0_ffn_w_down"}


def kernel(**inputs):
    import concourse.bacc as bacc
    from concourse.bass_utils import run_bass_kernel_spmd

    arrays = {k: np.ascontiguousarray(inputs[name]) for k, name in _INS.items()}
    B, T, E = arrays["x"].shape
    place = np.arange(T, dtype=np.float64)
    by_block = place.reshape(T // P, P)
    seen = np.arange(P)[:, None] <= np.arange(P)[None, :]
    arrays["causal_decay"] = np.where(seen[:, None, :], (DECAY ** by_block)[None], 0.0).astype(np.float32)
    arrays["query_decay"] = np.broadcast_to(DECAY ** place[P:], (P, T - P)).astype(np.float32)
    arrays["value_decay"] = np.ascontiguousarray(((1.0 - DECAY) * DECAY ** -by_block).T.astype(np.float32))

    nc = bacc.Bacc("TRN2", target_bir_lowering=False, num_devices=1)
    args = {k: nc.dram_tensor(f"in_{k}", a.shape, mybir.dt.from_np(a.dtype), kind="ExternalInput").ap() for k, a in arrays.items()}
    y = nc.dram_tensor("out_y", (B, T, E), F32, kind="ExternalOutput").ap()
    build(nc, out=y, **args)
    r = run_bass_kernel_spmd(nc, [{f"in_{k}": a for k, a in arrays.items()}], core_ids=[0])
    return r.results[0]["out_y"]
```

```python
from contextlib import ExitStack

import numpy as np

import concourse.bass as bass
from concourse import mybir

F32 = mybir.dt.float32
F32R = mybir.dt.float32r
I32 = mybir.dt.int32
ALU = mybir.AluOpType
ACT = mybir.ActivationFunctionType

P = 128
EPS = 1e-5
DECAY = 0.99
SCALE = 1.0 / 127.0
WARM_UP = 24


def build(nc, x, attn_w, ffn_w, decay, out):
    B, T, E = x.shape
    HID = ffn_w.shape[2]
    NB = T // P
    NH = HID // P
    LB = NB - 1
    assert E == P and T == 512 and HID % P == 0

    with ExitStack() as ctx:
        def sb(name, shape, dt=F32):
            return ctx.enter_context(nc.sbuf_tensor(name, shape, dt))

        def psum(name):
            return ctx.enter_context(nc.psum_tensor(name, [P, T], F32))

        def sem(name):
            return ctx.enter_context(nc.semaphore(name))

        identity = sb("identity", [P, P])
        ones = sb("ones", [P, 1])
        eps = sb("eps", [P, NB])
        minus_half = sb("minus_half", [P, NB])
        attn_f = sb("attn_f", [P, 4 * P + 2])
        wq_f, wk_f, wvT, wo_f = (attn_f[:, i * P:(i + 1) * P] for i in range(4))
        bq_c, bk_c = attn_f[:, 4 * P:4 * P + 1], attn_f[:, 4 * P + 1:4 * P + 2]
        qk_hi = sb("qk_hi", [P, 2, P], F32R)
        qk_lo = sb("qk_lo", [P, 2, P], F32R)
        wvo = sb("wvo", [P, P])
        ffn_int = sb("ffn_int", [P, 3, HID], I32)
        ffn_hi = sb("ffn_hi", [P, 3, HID], F32R)
        ffn_lo = sb("ffn_lo", [P, 3, HID], F32R)
        lo_abs = sb("lo_abs", [P, 3 * HID])
        lo_sum = sb("lo_sum", [P, 1])
        has_lo = sb("has_lo", [1, 1], I32)
        decay_t = sb("decay_t", [P, T + LB * P + NB])
        mask = decay_t[:, 0:T].rearrange("p (n t) -> p n t", t=P)
        q_dec = decay_t[:, T:T + LB * P]
        v_dec = decay_t[:, T + LB * P:]

        x_all = sb("x_all", [P, B * NB, P])
        stats = sb("stats", [P, NB, 6])
        mean_var = sb("mean_var", [P, NB, 2])
        var_eps = sb("var_eps", [P, NB])
        rstd = sb("rstd", [P, NB])
        xn = sb("xn", [P, NB, P])
        xT = sb("xT", [P, T])
        xT_hi = sb("xT_hi", [P, T], F32R)
        xT_lo = sb("xT_lo", [P, T], F32R)
        qT = sb("qT", [P, T])
        kT = sb("kT", [P, T])
        q_state = sb("q_state", [P, LB * P])
        k_tok = sb("k_tok", [P, LB, P])
        v_tok = sb("v_tok", [P, NB, P])
        att = sb("att", [P, NB, P])
        kv = sb("kv", [P, LB, P])
        state = sb("state", [P, LB - 1, P])
        sig_g = sb("sig_g", [P, NH, T])
        silu_g = sb("silu_g", [P, NH, T])
        h = sb("h", [P, NH, T])
        h_hi = sb("h_hi", [P, NH, T], F32R)
        h_lo = sb("h_lo", [P, NH, T], F32R)
        oT = sb("oT", [P, T])
        y_out = sb("y_out", [P, NB, P])

        ps_t = psum("ps_t")
        ps_q = psum("ps_q")
        ps_k = psum("ps_k")
        ps_v = psum("ps_v")
        ps_g = psum("ps_g")
        ps_u = psum("ps_u")
        ps_a = psum("ps_a")
        ps_o = psum("ps_o")
        gate_bank = [ps_g, ps_q, ps_g]
        up_bank = [ps_u, ps_k, ps_u]

        attn_w_loaded = sem("attn_w_loaded")
        ffn_w_loaded = sem("ffn_w_loaded")
        decay_loaded = sem("decay_loaded")
        blank_ready = sem("blank_ready")
        identity_ready = sem("identity_ready")
        norm_consts_ready = sem("norm_consts_ready")
        wvo_psum_ready = sem("wvo_psum_ready")
        wvo_ready = sem("wvo_ready")
        qk_hi_ready = sem("qk_hi_ready")
        qk_lo_ready = sem("qk_lo_ready")
        ffn_hi_ready = sem("ffn_hi_ready")
        ffn_lo_ready = sem("ffn_lo_ready")
        lo_sum_ready = sem("lo_sum_ready")
        lo_total_ready = sem("lo_total_ready")
        has_lo_ready = sem("has_lo_ready")
        x_loaded = sem("x_loaded")
        stats_ready = sem("stats_ready")
        mean_var_ready = sem("mean_var_ready")
        var_eps_ready = sem("var_eps_ready")
        rstd_ready = sem("rstd_ready")
        xn_ready = sem("xn_ready")
        xT_psum_ready = sem("xT_psum_ready")
        xT_hi_ready = sem("xT_hi_ready")
        xT_lo_ready = sem("xT_lo_ready")
        xT_ready = sem("xT_ready")
        q_psum_ready = sem("q_psum_ready")
        k_psum_ready = sem("k_psum_ready")
        q_ready = sem("q_ready")
        k_ready = sem("k_ready")
        q_state_ready = sem("q_state_ready")
        v_psum_ready = sem("v_psum_ready")
        v_ready = sem("v_ready")
        att_psum_ready = sem("att_psum_ready")
        att_ready = sem("att_ready")
        k_tok_psum_ready = sem("k_tok_psum_ready")
        k_tok_ready = sem("k_tok_ready")
        kv_psum_ready = sem("kv_psum_ready")
        kv_ready = sem("kv_ready")
        state_ready = sem("state_ready")
        gate_psum_ready = sem("gate_psum_ready")
        up_psum_ready = sem("up_psum_ready")
        sig_g_ready = sem("sig_g_ready")
        silu_ready = sem("silu_ready")
        h_ready = sem("h_ready")
        h_hi_ready = sem("h_hi_ready")
        h_lo_pool_ready = sem("h_lo_pool_ready")
        h_lo_dve_ready = sem("h_lo_dve_ready")
        oT_psum_ready = sem("oT_psum_ready")
        oT_ready = sem("oT_ready")
        out_psum_ready = sem("out_psum_ready")
        y_ready = sem("y_ready")
        y_stored = sem("y_stored")

        x_blocks = x.rearrange("b (n p) e -> b p n e", p=P)
        out_blocks = out.rearrange("b (n p) e -> b p n e", p=P)

        block = ctx.enter_context(nc.Block())

        @block.sync
        def _(sp):
            def load_x(b):
                sp.dma_start(x_all[:, bass.ds(b * NB, NB), :], x_blocks[b]).then_inc(x_loaded, 16)

            def store_y(b):
                sp.wait_ge(y_ready, b + 1)
                sp.dma_start(out_blocks[b], y_out[:, :, :]).then_inc(y_stored, 16)

            load_x(0)
            sp.dma_start(ffn_int[:], ffn_w).then_inc(ffn_w_loaded, 16)
            with sp.Fori(1, B) as b:
                sp.wait_ge(x_loaded, b * 16)
                load_x(b)
            with sp.Fori(0, B) as b:
                store_y(b)
            sp.wait_ge(y_stored, 16 * B)

        @block.gpsimd
        def _(pool):
            nc.gpsimd.memset(identity[:], 0.0).then_inc(blank_ready, 1)
            nc.gpsimd.memset(ones[:], 1.0)
            nc.gpsimd.memset(eps[:], EPS)
            nc.gpsimd.memset(minus_half[:], -0.5).then_inc(norm_consts_ready, 1)
            pool.wait_ge(blank_ready, 1)
            nc.gpsimd.affine_select(out=identity[:], in_=identity[:], compare_op=ALU.not_equal, fill=1.0,
                                    base=0, pattern=[[-1, P]], channel_multiplier=1).then_inc(identity_ready, 1)

            def rsqrt_var(b):
                pool.wait_ge(mean_var_ready, b + 1)
                nc.gpsimd.tensor_tensor(var_eps[:], mean_var[:, :, 1], eps[:], ALU.add).then_inc(var_eps_ready, 1)
                pool.wait_ge(var_eps_ready, b + 1)
                nc.gpsimd.tensor_tensor(rstd[:], var_eps[:], minus_half[:], ALU.pow).then_inc(rstd_ready, 1)

            def whole_xT(b):
                pool.wait_ge(xT_lo_ready, b + 1)
                nc.gpsimd.tensor_tensor(xT[:], xT_hi[:].bitcast(F32), xT_lo[:].bitcast(F32), ALU.add).then_inc(xT_ready, 1)

            def low_h(b, c):
                pool.wait_ge(h_hi_ready, b * NH + c + 1)
                nc.gpsimd.tensor_tensor(h_lo[:, c], h[:, c], h_hi[:, c].bitcast(F32),
                                        ALU.subtract).then_inc(h_lo_pool_ready, 1)

            def sum_state(b):
                pool.wait_ge(kv_ready, b + 1)
                nc.gpsimd.tensor_tensor(state[:, 0], kv[:, 0], kv[:, 1], ALU.add).then_inc(state_ready, 1)
                for n in range(1, LB - 1):
                    pool.wait_ge(state_ready, b * (LB - 1) + n)
                    nc.gpsimd.tensor_tensor(state[:, n], state[:, n - 1], kv[:, n + 1], ALU.add).then_inc(state_ready, 1)

            def sequence(b, left):
                pool.wait_ge(q_ready, b + 1)
                nc.gpsimd.tensor_tensor(q_state[:], qT[:, P:T], q_dec, ALU.mult).then_inc(q_state_ready, 1)
                low_h(b, 0)
                if left >= 2:
                    rsqrt_var(b + 2)
                low_h(b, 1)
                sum_state(b)
                if left >= 1:
                    whole_xT(b + 1)

            pool.wait_ge(norm_consts_ready, 1)
            rsqrt_var(0)
            rsqrt_var(1)
            whole_xT(0)
            pool.wait_ge(decay_loaded, 16)
            sequence(0, left=B - 1)
            with pool.Fori(1, B - 2) as b:
                sequence(b, left=2)
            sequence(B - 2, left=1)
            sequence(B - 1, left=0)

        @block.scalar
        def _(act):
            act.dma_start(attn_f[:], attn_w).then_inc(attn_w_loaded, 16)
            act.dma_start(decay_t[:], decay).then_inc(decay_loaded, 16)

            def copy_xT(b):
                act.wait_ge(xT_psum_ready, b + 1)
                nc.scalar.copy(xT_hi[:], ps_t[:]).then_inc(xT_hi_ready, 1)

            def sigmoid_gate(b, c):
                act.wait_ge(gate_psum_ready, b * NH + c + 1)
                nc.scalar.activation(sig_g[:, c], gate_bank[c][:], ACT.Sigmoid, scale=SCALE).then_inc(sig_g_ready, 1)

            def round_h(b, c):
                act.wait_ge(h_ready, b * NH + c + 1)
                nc.scalar.copy(h_hi[:, c], h[:, c]).then_inc(h_hi_ready, 1)

            def copy_oT(b):
                act.wait_ge(oT_psum_ready, b + 1)
                nc.scalar.copy(oT[:], ps_o[:]).then_inc(oT_ready, 1)

            def sequence(b, last=False):
                act.wait_ge(q_psum_ready, b + 1)
                nc.scalar.activation(qT[:], ps_q[:], ACT.Sigmoid, bias=bq_c).then_inc(q_ready, 1)
                act.wait_ge(k_psum_ready, b + 1)
                nc.scalar.activation(kT[:], ps_k[:], ACT.Sigmoid, bias=bk_c).then_inc(k_ready, 1)
                sigmoid_gate(b, 0)
                act.wait_ge(v_psum_ready, b + 1)
                for n in range(NB):
                    nc.scalar.activation(v_tok[:, n], ps_v[:, n * P:(n + 1) * P], ACT.Copy,
                                         scale=v_dec[:, n:n + 1]).then_inc(v_ready, 1)
                round_h(b, 0)
                sigmoid_gate(b, 1)
                act.wait_ge(k_tok_psum_ready, b + 1)
                nc.scalar.copy(k_tok[:].rearrange("p n e -> p (n e)"), ps_t[:, 0:LB * P]).then_inc(k_tok_ready, 1)
                sigmoid_gate(b, 2)
                round_h(b, 1)
                act.wait_ge(kv_psum_ready, b + 1)
                nc.scalar.copy(kv[:].rearrange("p n e -> p (n e)"), ps_v[:, 0:LB * P]).then_inc(kv_ready, 1)
                if not last:
                    copy_xT(b + 1)
                round_h(b, 2)
                copy_oT(b)

            act.wait_ge(norm_consts_ready, 1)
            nc.scalar.activation(lo_sum[:], ones[:], ACT.Sigmoid)
            act.wait_ge(attn_w_loaded, 16)
            nc.scalar.copy(qk_hi[:].rearrange("p m e -> p (m e)"), attn_f[:, 0:2 * P]).then_inc(qk_hi_ready, 1)
            act.wait_ge(ffn_w_loaded, 16)
            nc.scalar.copy(ffn_hi[:], ffn_int[:]).then_inc(ffn_hi_ready, 1)
            act.wait_ge(wvo_psum_ready, 1)
            nc.scalar.copy(wvo[:], ps_a[:, 0:P]).then_inc(wvo_ready, 1)
            act.wait_ge(ffn_lo_ready, 1)
            nc.scalar.activation(lo_abs[:], ffn_lo[:].rearrange("p m e -> p (m e)").bitcast(F32), ACT.Abs,
                                 accum_out=lo_sum[:]).then_inc(lo_sum_ready, 1)
            copy_xT(0)
            act.wait_ge(decay_loaded, 16)
            sequence(0)
            with act.Fori(1, B - 1) as b:
                sequence(b)
            sequence(B - 1, last=True)

        @block.vector
        def _(dve):
            def norm_stats(b):
                dve.wait_ge(x_loaded, (b + 1) * 16)
                for n in range(NB):
                    nc.vector.bn_stats(stats[:, n], x_all[:, b * NB + n, :]).then_inc(stats_ready, 1)

            def norm_aggregate(b):
                for n in range(NB):
                    last = nc.vector.bn_aggr(mean_var[:, n], stats[:, n])
                last.then_inc(mean_var_ready, 1)

            def norm_apply(b):
                dve.wait_ge(mean_var_ready, b + 1)
                dve.wait_ge(rstd_ready, b + 1)
                for n in range(NB):
                    nc.vector.tensor_scalar(xn[:, n], x_all[:, b * NB + n, :], mean_var[:, n, 0:1], rstd[:, n:n + 1],
                                            ALU.subtract, ALU.mult).then_inc(xn_ready, 1)

            def subtract_xT(b):
                dve.wait_ge(xT_hi_ready, b + 1)
                nc.vector.tensor_tensor(xT_lo[:], ps_t[:], xT_hi[:].bitcast(F32), ALU.subtract).then_inc(xT_lo_ready, 1)

            def residual(b):
                dve.wait_ge(out_psum_ready, b + 1)
                if not isinstance(b, int) or b > 0:
                    dve.wait_ge(y_stored, b * 16)
                nc.vector.tensor_tensor(y_out[:], ps_t[:].rearrange("p (n e) -> p n e", e=E),
                                        x_all[:, bass.ds(b * NB, NB), :], ALU.add).then_inc(y_ready, 1)

            def hidden(b, c):
                dve.wait_ge(sig_g_ready, b * NH + c + 1)
                nc.vector.scalar_tensor_tensor(silu_g[:, c], gate_bank[c][:], SCALE, sig_g[:, c],
                                               ALU.mult, ALU.mult).then_inc(silu_ready, 1)
                dve.wait_ge(silu_ready, b * NH + c + 1)
                dve.wait_ge(up_psum_ready, b * NH + c + 1)
                nc.vector.scalar_tensor_tensor(h[:, c], up_bank[c][:], SCALE * SCALE, silu_g[:, c],
                                               ALU.mult, ALU.mult).then_inc(h_ready, 1)

            def sequence(b, left, first=False):
                if left >= 1:
                    norm_apply(b + 1)
                if not first:
                    residual(b - 1)
                if left >= 2:
                    norm_stats(b + 2)
                    dve.wait_ge(stats_ready, (b + 3) * NB)
                hidden(b, 0)
                if left >= 2:
                    norm_aggregate(b + 2)
                dve.wait_ge(att_psum_ready, b + 1)
                nc.vector.tensor_tensor(att[:], ps_a[:].rearrange("p (n t) -> p n t", t=P), mask,
                                        ALU.mult).then_inc(att_ready, 1)
                hidden(b, 1)
                hidden(b, 2)
                if left >= 1:
                    subtract_xT(b + 1)
                dve.wait_ge(h_hi_ready, (b + 1) * NH)
                nc.vector.tensor_tensor(h_lo[:, NH - 1], h[:, NH - 1], h_hi[:, NH - 1].bitcast(F32),
                                        ALU.subtract).then_inc(h_lo_dve_ready, 1)

            norm_stats(0)
            dve.wait_ge(stats_ready, NB)
            norm_aggregate(0)
            dve.wait_ge(qk_hi_ready, 1)
            nc.vector.tensor_tensor(qk_lo[:].rearrange("p m e -> p (m e)"), attn_f[:, 0:2 * P],
                                    qk_hi[:].rearrange("p m e -> p (m e)").bitcast(F32), ALU.subtract).then_inc(qk_lo_ready, 1)
            norm_apply(0)
            dve.wait_ge(ffn_hi_ready, 1)
            nc.vector.tensor_tensor(ffn_lo[:], ffn_int[:], ffn_hi[:].bitcast(F32), ALU.subtract).then_inc(ffn_lo_ready, 1)
            subtract_xT(0)
            dve.wait_ge(lo_total_ready, 1)
            nc.vector.tensor_scalar(has_lo[:], ps_k[0:1, 0:1], 0.0, None, ALU.is_gt).then_inc(has_lo_ready, 1)
            norm_stats(1)
            dve.wait_ge(stats_ready, 2 * NB)
            norm_aggregate(1)
            dve.wait_ge(decay_loaded, 16)
            sequence(0, left=B - 1, first=True)
            with dve.Fori(1, B - 2) as b:
                sequence(b, left=2)
            sequence(B - 2, left=1)
            sequence(B - 1, left=0)
            residual(B - 1)

        @block.tensor
        def _(pe):
            def split_product(bank, w_hi, w_lo, x_hi, x_lo, start=True, stop=True):
                nc.tensor.matmul(bank[:], w_hi, x_hi, start=start, stop=False)
                last = nc.tensor.matmul(bank[:], w_hi, x_lo, start=False, stop=stop and w_lo is None)
                if w_lo is not None:
                    last = nc.tensor.matmul(bank[:], w_lo, x_hi, start=False, stop=stop)
                return last

            def transpose_xn(b, by_block=False):
                if not by_block:
                    pe.wait_ge(xn_ready, (b + 1) * NB)
                for n in range(NB):
                    if by_block:
                        pe.wait_ge(xn_ready, b * NB + n + 1)
                    last = nc.tensor.transpose(ps_t[:, n * P:(n + 1) * P], xn[:, n], identity[:])
                last.then_inc(xT_psum_ready, 1)

            def transpose_out(b):
                pe.wait_ge(oT_ready, b + 1)
                for n in range(NB):
                    last = nc.tensor.transpose(ps_t[:, n * P:(n + 1) * P], oT[:, n * P:(n + 1) * P], identity[:])
                last.then_inc(out_psum_ready, 1)

            def sequences(with_lo):
                def weight(m, c):
                    chunk = slice(c * P, (c + 1) * P)
                    return ffn_hi[:, m, chunk], ffn_lo[:, m, chunk] if with_lo else None

                def gate_up(b, c):
                    split_product(gate_bank[c], *weight(0, c), xT_hi[:], xT_lo[:]).then_inc(gate_psum_ready, 1)
                    split_product(up_bank[c], *weight(1, c), xT_hi[:], xT_lo[:]).then_inc(up_psum_ready, 1)

                def down(b, c, stop=False):
                    if c < NH - 1:
                        pe.wait_ge(h_lo_pool_ready, b * (NH - 1) + c + 1)
                    else:
                        pe.wait_ge(h_lo_dve_ready, b + 1)
                    return split_product(ps_o, *weight(2, c), h_hi[:, c], h_lo[:, c], start=False, stop=stop)

                def sequence(b, first=False, last=False):
                    pe.wait_ge(xT_hi_ready, b + 1)
                    pe.wait_ge(xT_lo_ready, b + 1)
                    split_product(ps_q, qk_hi[:, 0], qk_lo[:, 0], xT_hi[:], xT_lo[:]).then_inc(q_psum_ready, 1)
                    split_product(ps_k, qk_hi[:, 1], qk_lo[:, 1], xT_hi[:], xT_lo[:]).then_inc(k_psum_ready, 1)
                    if not first:
                        transpose_out(b - 1)
                    gate_up(b, 0)
                    pe.wait_ge(xT_ready, b + 1)
                    for n in range(NB):
                        mm = nc.tensor.matmul(ps_v[:, n * P:(n + 1) * P], xT[:, n * P:(n + 1) * P], wvo[:], start=True, stop=True)
                    mm.then_inc(v_psum_ready, 1)
                    pe.wait_ge(q_ready, b + 1)
                    pe.wait_ge(k_ready, b + 1)
                    for n in range(NB):
                        mm = nc.tensor.matmul(ps_a[:, n * P:(n + 1) * P], kT[:, n * P:(n + 1) * P], qT[:, n * P:(n + 1) * P],
                                              start=True, stop=True)
                    mm.then_inc(att_psum_ready, 1)
                    gate_up(b, 1)
                    if not first:
                        pe.wait_ge(y_ready, b)
                    for n in range(LB):
                        mm = nc.tensor.transpose(ps_t[:, n * P:(n + 1) * P], kT[:, n * P:(n + 1) * P], identity[:])
                    mm.then_inc(k_tok_psum_ready, 1)
                    pe.wait_ge(h_ready, b * NH + 1)
                    gate_up(b, 2)
                    pe.wait_ge(k_tok_ready, b + 1)
                    pe.wait_ge(v_ready, (b + 1) * NB)
                    for n in range(LB):
                        mm = nc.tensor.matmul(ps_v[:, n * P:(n + 1) * P], k_tok[:, n], v_tok[:, n], start=True, stop=True)
                    mm.then_inc(kv_psum_ready, 1)
                    if not last:
                        transpose_xn(b + 1)
                    pe.wait_ge(att_ready, b + 1)
                    for n in range(NB):
                        nc.tensor.matmul(ps_o[:, n * P:(n + 1) * P], v_tok[:, n], att[:, n], start=(n == 0), stop=False)
                    for c in range(NH - 1):
                        down(b, c)
                    pe.wait_ge(q_state_ready, b + 1)
                    pe.wait_ge(kv_ready, b + 1)
                    for n in range(LB):
                        if n >= 1:
                            pe.wait_ge(state_ready, b * (LB - 1) + n)
                        nc.tensor.matmul(ps_o[:, (n + 1) * P:(n + 2) * P], kv[:, 0] if n == 0 else state[:, n - 1],
                                         q_state[:, n * P:(n + 1) * P], start=False, stop=False)
                    down(b, NH - 1, stop=True).then_inc(oT_psum_ready, 1)

                sequence(0, first=True)
                with pe.Fori(1, B - 1) as b:
                    sequence(b)
                sequence(B - 1, last=True)
                transpose_out(B - 1)

            pe.wait_ge(identity_ready, 1)
            for n in range(WARM_UP):
                nc.tensor.matmul(ps_a[:, 0:P], identity[:], identity[:], start=True, stop=True)
            pe.wait_ge(attn_w_loaded, 16)
            nc.tensor.matmul(ps_a[:, 0:P], wvT, wo_f, start=True, stop=True).then_inc(wvo_psum_ready, 1)
            transpose_xn(0, by_block=True)
            pe.wait_ge(norm_consts_ready, 1)
            pe.wait_ge(lo_sum_ready, 1)
            nc.tensor.matmul(ps_k[0:1, 0:1], lo_sum[:], ones[:], start=True, stop=True).then_inc(lo_total_ready, 1)
            pe.wait_ge(wvo_ready, 1)
            pe.wait_ge(qk_lo_ready, 1)
            pe.wait_ge(has_lo_ready, 1)
            has = pe.value_load(has_lo[0:1, 0:1], min_val=0, max_val=1)
            with pe.If(has > 0):
                sequences(with_lo=True)
            with pe.Else():
                sequences(with_lo=False)


def kernel(**inputs):
    import concourse.bacc as bacc
    from concourse.bass_utils import run_bass_kernel_spmd

    given = {k: np.asarray(v) for k, v in inputs.items()}
    x = np.ascontiguousarray(given["L0_attn_x"])
    B, T, E = x.shape
    HID = given["L0_ffn_w_gate"].shape[0]
    attn_w = np.concatenate([given["L0_attn_Wq"], given["L0_attn_Wk"], given["L0_attn_Wv"].T, given["L0_attn_Wo"],
                             given["L0_attn_bq"][:, None], given["L0_attn_bk"][:, None]], axis=1)
    down = given["L0_ffn_w_down"].T.reshape(HID // P, P, E).transpose(1, 0, 2).reshape(P, HID)
    ffn_w = np.stack([given["L0_ffn_w_gate"].T, given["L0_ffn_w_up"].T, down], axis=1)
    place = np.arange(T, dtype=np.float64)
    by_block = place.reshape(T // P, P)
    seen = np.arange(P)[:, None] <= np.arange(P)[None, :]
    decay = np.concatenate([np.where(seen[:, None, :], (DECAY ** by_block)[None], 0.0).reshape(P, T),
                            np.broadcast_to(DECAY ** place[P:], (P, T - P)),
                            ((1.0 - DECAY) * DECAY ** -by_block).T], axis=1).astype(np.float32)
    arrays = {"x": x, "attn_w": attn_w, "ffn_w": ffn_w, "decay": decay}

    nc = bacc.Bacc("TRN2", target_bir_lowering=False, num_devices=1)
    args = {k: nc.dram_tensor(f"in_{k}", a.shape, mybir.dt.from_np(a.dtype), kind="ExternalInput").ap() for k, a in arrays.items()}
    y = nc.dram_tensor("out_y", (B, T, E), F32, kind="ExternalOutput").ap()
    build(nc, out=y, **args)
    r = run_bass_kernel_spmd(nc, [{f"in_{k}": np.ascontiguousarray(a) for k, a in arrays.items()}], core_ids=[0])
    return r.results[0]["out_y"]
```

```python
from contextlib import ExitStack

import numpy as np

import concourse.bass as bass
from concourse import mybir

F32 = mybir.dt.float32
F32R = mybir.dt.float32r
I32 = mybir.dt.int32
ALU = mybir.AluOpType
ACT = mybir.ActivationFunctionType

P = 128
EPS = 1e-5
DECAY = 0.99
SCALE = 1.0 / 127.0


def build(nc, x, attn_w, ffn_w, decay, out):
    B, T, E = x.shape
    HID = ffn_w.shape[2]
    NB = T // P
    NH = HID // P
    LB = NB - 1
    assert E == P and T == 512 and HID == 3 * P

    with ExitStack() as ctx:
        def sb(name, shape, dt=F32):
            return ctx.enter_context(nc.sbuf_tensor(name, shape, dt))

        def psum(name):
            return ctx.enter_context(nc.psum_tensor(name, [P, T], F32))

        def sem(name):
            return ctx.enter_context(nc.semaphore(name))

        identity = sb("identity", [P, P])
        ones = sb("ones", [P, 1])
        eps = sb("eps", [P, NB])
        minus_half = sb("minus_half", [P, NB])
        attn_f = sb("attn_f", [P, 4 * P + 2])
        wq_f, wk_f, wvT, wo_f = (attn_f[:, i * P:(i + 1) * P] for i in range(4))
        bq_c, bk_c = attn_f[:, 4 * P:4 * P + 1], attn_f[:, 4 * P + 1:4 * P + 2]
        qk_hi = sb("qk_hi", [P, 2, P], F32R)
        qk_lo = sb("qk_lo", [P, 2, P], F32R)
        wvo = sb("wvo", [P, P])
        ffn_int = sb("ffn_int", [P, 3, HID], I32)
        ffn_hi = sb("ffn_hi", [P, 3, HID], F32R)
        ffn_lo = sb("ffn_lo", [P, 3, HID], F32R)
        lo_abs = sb("lo_abs", [P, 3, HID])
        lo_sum = sb("lo_sum", [P, 3])
        warm = sb("warm", [P, 1])
        has_lo = sb("has_lo", [1, 1], I32)
        decay_t = sb("decay_t", [P, T + LB * P + NB])
        mask = decay_t[:, 0:T].rearrange("p (n t) -> p n t", t=P)
        q_dec = decay_t[:, T:T + LB * P]
        v_dec = decay_t[:, T + LB * P:]

        x_all = sb("x_all", [P, B * NB, P])
        stats = sb("stats", [P, NB, 6])
        mean_var = sb("mean_var", [P, NB, 2])
        var_eps = sb("var_eps", [P, NB])
        rstd = sb("rstd", [P, NB])
        xn = sb("xn", [P, NB, P])
        xT = sb("xT", [P, T])
        xT_hi = sb("xT_hi", [P, T], F32R)
        xT_lo = sb("xT_lo", [P, T], F32R)
        qT = sb("qT", [P, T])
        kT = sb("kT", [P, T])
        q_state = sb("q_state", [P, LB * P])
        k_tok = sb("k_tok", [P, LB, P])
        v_tok = sb("v_tok", [P, NB, P])
        att = sb("att", [P, NB, P])
        kv = sb("kv", [P, LB, P])
        state = sb("state", [P, LB - 1, P])
        sig_g = sb("sig_g", [P, NH, T])
        silu_g = sb("silu_g", [P, NH, T])
        h = sb("h", [P, NH, T])
        h_hi = sb("h_hi", [P, NH, T], F32R)
        h_lo = sb("h_lo", [P, NH, T], F32R)
        oT = sb("oT", [P, T])
        y_out = sb("y_out", [P, NB, P])

        ps_t = psum("ps_t")
        ps_q = psum("ps_q")
        ps_k = psum("ps_k")
        ps_v = psum("ps_v")
        ps_g = psum("ps_g")
        ps_u = psum("ps_u")
        ps_a = psum("ps_a")
        ps_o = psum("ps_o")
        gate_bank = [ps_g, ps_q, ps_g]
        up_bank = [ps_u, ps_k, ps_u]

        attn_w_loaded = sem("attn_w_loaded")
        ffn_w_loaded = [sem(f"ffn_w{m}_loaded") for m in range(3)]
        decay_loaded = sem("decay_loaded")
        blank_ready = sem("blank_ready")
        identity_ready = sem("identity_ready")
        norm_consts_ready = sem("norm_consts_ready")
        wvo_psum_ready = sem("wvo_psum_ready")
        wvo_ready = sem("wvo_ready")
        qk_hi_ready = sem("qk_hi_ready")
        qk_lo_ready = sem("qk_lo_ready")
        ffn_hi_ready = sem("ffn_hi_ready")
        ffn_lo_ready = sem("ffn_lo_ready")
        lo_sum_ready = sem("lo_sum_ready")
        lo_total_ready = sem("lo_total_ready")
        has_lo_ready = sem("has_lo_ready")
        x_loaded = sem("x_loaded")
        stats_ready = sem("stats_ready")
        mean_var_ready = sem("mean_var_ready")
        var_eps_ready = sem("var_eps_ready")
        rstd_ready = sem("rstd_ready")
        xn_ready = sem("xn_ready")
        xT_psum_ready = sem("xT_psum_ready")
        xT_hi_ready = sem("xT_hi_ready")
        xT_lo_ready = sem("xT_lo_ready")
        xT_ready = sem("xT_ready")
        q_psum_ready = sem("q_psum_ready")
        k_psum_ready = sem("k_psum_ready")
        q_ready = sem("q_ready")
        k_ready = sem("k_ready")
        q_state_ready = sem("q_state_ready")
        v_psum_ready = sem("v_psum_ready")
        v_ready = sem("v_ready")
        att_psum_ready = sem("att_psum_ready")
        att_ready = sem("att_ready")
        k_tok_psum_ready = sem("k_tok_psum_ready")
        k_tok_ready = sem("k_tok_ready")
        kv_psum_ready = sem("kv_psum_ready")
        kv_ready = sem("kv_ready")
        state_ready = sem("state_ready")
        gate_psum_ready = sem("gate_psum_ready")
        up_psum_ready = sem("up_psum_ready")
        sig_g_ready = sem("sig_g_ready")
        silu_ready = sem("silu_ready")
        h_ready = sem("h_ready")
        h_hi_ready = sem("h_hi_ready")
        h_lo_ready = [sem(f"h_lo{c}_ready") for c in range(NH)]
        oT_psum_ready = sem("oT_psum_ready")
        oT_ready = sem("oT_ready")
        out_psum_ready = sem("out_psum_ready")
        y_ready = sem("y_ready")
        y_stored = sem("y_stored")

        x_blocks = x.rearrange("b (n p) e -> b p n e", p=P)
        out_blocks = out.rearrange("b (n p) e -> b p n e", p=P)

        def column_parts(parts):
            return [slice(i * T // parts, (i + 1) * T // parts) for i in range(parts)]

        block = ctx.enter_context(nc.Block())

        @block.sync
        def _(sp):
            def load_x(b):
                sp.dma_start(x_all[:, bass.ds(b * NB, NB), :], x_blocks[b]).then_inc(x_loaded, 16)

            def store_y(b):
                sp.wait_ge(y_ready, b + 1)
                sp.dma_start(out_blocks[b], y_out[:, :, :]).then_inc(y_stored, 16)

            load_x(0)
            for m in range(3):
                sp.dma_start(ffn_int[:, m], ffn_w[:, m]).then_inc(ffn_w_loaded[m], 16)
            with sp.Fori(1, B) as b:
                sp.wait_ge(x_loaded, b * 16)
                load_x(b)
            with sp.Fori(0, B - 1) as b:
                store_y(b)
            for i in range(2):
                blocks = slice(i * NB // 2, (i + 1) * NB // 2)
                sp.wait_ge(y_ready, B + i)
                sp.dma_start(out_blocks[B - 1][:, blocks], y_out[:, blocks]).then_inc(y_stored, 16)
            sp.wait_ge(y_stored, 16 * (B + 1))

        @block.gpsimd
        def _(pool):
            nc.gpsimd.memset(identity[:], 0.0).then_inc(blank_ready, 1)
            nc.gpsimd.memset(ones[:], 1.0)
            nc.gpsimd.memset(eps[:], EPS)
            nc.gpsimd.memset(minus_half[:], -0.5).then_inc(norm_consts_ready, 1)
            pool.wait_ge(blank_ready, 1)
            nc.gpsimd.affine_select(out=identity[:], in_=identity[:], compare_op=ALU.not_equal, fill=1.0,
                                    base=0, pattern=[[-1, P]], channel_multiplier=1).then_inc(identity_ready, 1)

            def rsqrt_var(b):
                pool.wait_ge(mean_var_ready, b + 1)
                nc.gpsimd.tensor_tensor(var_eps[:], mean_var[:, :, 1], eps[:], ALU.add).then_inc(var_eps_ready, 1)
                pool.wait_ge(var_eps_ready, b + 1)
                nc.gpsimd.tensor_tensor(rstd[:], var_eps[:], minus_half[:], ALU.pow).then_inc(rstd_ready, 1)

            def whole_xT(b):
                pool.wait_ge(xT_lo_ready, b + 1)
                nc.gpsimd.tensor_tensor(xT[:], xT_hi[:].bitcast(F32), xT_lo[:].bitcast(F32), ALU.add).then_inc(xT_ready, 1)

            def low_h(b, c):
                pool.wait_ge(h_hi_ready, b * NH + c + 1)
                nc.gpsimd.tensor_tensor(h_lo[:, c], h[:, c], h_hi[:, c].bitcast(F32),
                                        ALU.subtract).then_inc(h_lo_ready[c], 1)

            def sum_state(b):
                pool.wait_ge(kv_ready, b + 1)
                nc.gpsimd.tensor_tensor(state[:, 0], kv[:, 0], kv[:, 1], ALU.add).then_inc(state_ready, 1)
                for n in range(1, LB - 1):
                    pool.wait_ge(state_ready, b * (LB - 1) + n)
                    nc.gpsimd.tensor_tensor(state[:, n], state[:, n - 1], kv[:, n + 1], ALU.add).then_inc(state_ready, 1)

            def sequence(b, left):
                pool.wait_ge(q_ready, b + 1)
                if not isinstance(b, int) or b > 0:
                    pool.wait_ge(oT_psum_ready, b)
                nc.gpsimd.tensor_tensor(q_state[:], qT[:, P:T], q_dec, ALU.mult).then_inc(q_state_ready, 1)
                if left >= 2:
                    rsqrt_var(b + 2)
                if left >= 1:
                    low_h(b, 1)
                sum_state(b)
                if left >= 1:
                    whole_xT(b + 1)

            pool.wait_ge(norm_consts_ready, 1)
            rsqrt_var(0)
            whole_xT(0)
            rsqrt_var(1)
            pool.wait_ge(decay_loaded, 16)
            sequence(0, left=B - 1)
            with pool.Fori(1, B - 2) as b:
                sequence(b, left=2)
            sequence(B - 2, left=1)
            sequence(B - 1, left=0)

        @block.scalar
        def _(act):
            act.dma_start(attn_f[:], attn_w).then_inc(attn_w_loaded, 16)
            act.dma_start(decay_t[:], decay).then_inc(decay_loaded, 16)

            def copy_xT(b):
                act.wait_ge(xT_psum_ready, b + 1)
                nc.scalar.copy(xT_hi[:], ps_t[:]).then_inc(xT_hi_ready, 1)

            def sigmoid_gate(b, c):
                act.wait_ge(gate_psum_ready, b * NH + c + 1)
                nc.scalar.activation(sig_g[:, c], gate_bank[c][:], ACT.Sigmoid, scale=SCALE).then_inc(sig_g_ready, 1)

            def round_h(b, c):
                act.wait_ge(h_ready, b * NH + c + 1)
                nc.scalar.copy(h_hi[:, c], h[:, c]).then_inc(h_hi_ready, 1)

            def copy_oT(b, parts=1):
                act.wait_ge(oT_psum_ready, b + 1)
                for cols in column_parts(parts):
                    nc.scalar.copy(oT[:, cols], ps_o[:, cols]).then_inc(oT_ready, 1)

            def sigmoid_qk(b):
                act.wait_ge(q_psum_ready, b + 1)
                if not isinstance(b, int) or b > 0:
                    act.wait_ge(q_state_ready, b)
                nc.scalar.activation(qT[:], ps_q[:], ACT.Sigmoid, bias=bq_c).then_inc(q_ready, 1)
                act.wait_ge(k_psum_ready, b + 1)
                nc.scalar.activation(kT[:], ps_k[:], ACT.Sigmoid, bias=bk_c).then_inc(k_ready, 1)

            def sequence(b, last=False):
                sigmoid_gate(b, 0)
                sigmoid_gate(b, 1)
                act.wait_ge(v_psum_ready, b + 1)
                for n in range(NB):
                    nc.scalar.activation(v_tok[:, n], ps_v[:, n * P:(n + 1) * P], ACT.Copy,
                                         scale=v_dec[:, n:n + 1]).then_inc(v_ready, 1)
                act.wait_ge(k_tok_psum_ready, b + 1)
                nc.scalar.copy(k_tok[:].rearrange("p n e -> p (n e)"), ps_t[:, 0:LB * P]).then_inc(k_tok_ready, 1)
                round_h(b, 0)
                sigmoid_gate(b, 2)
                if not last:
                    copy_xT(b + 1)
                round_h(b, 1)
                act.wait_ge(kv_psum_ready, b + 1)
                nc.scalar.copy(kv[:].rearrange("p n e -> p (n e)"), ps_v[:, 0:LB * P]).then_inc(kv_ready, 1)
                round_h(b, 2)
                if not last:
                    sigmoid_qk(b + 1)
                copy_oT(b, parts=2 if last else 1)

            act.wait_ge(norm_consts_ready, 1)
            nc.scalar.activation(warm[:], ones[:], ACT.Sigmoid)
            act.wait_ge(attn_w_loaded, 16)
            nc.scalar.copy(qk_hi[:].rearrange("p m e -> p (m e)"), attn_f[:, 0:2 * P]).then_inc(qk_hi_ready, 1)

            def high_ffn(m):
                act.wait_ge(ffn_w_loaded[m], 16)
                nc.scalar.copy(ffn_hi[:, m], ffn_int[:, m]).then_inc(ffn_hi_ready, 1)

            def sum_low_ffn(m):
                act.wait_ge(ffn_lo_ready, m + 1)
                nc.scalar.activation(lo_abs[:, m], ffn_lo[:, m].bitcast(F32), ACT.Abs,
                                     accum_out=lo_sum[:, m:m + 1]).then_inc(lo_sum_ready, 1)

            high_ffn(0)
            sum_low_ffn(0)
            high_ffn(1)
            high_ffn(2)
            copy_xT(0)
            sum_low_ffn(1)
            sum_low_ffn(2)
            act.wait_ge(wvo_psum_ready, 1)
            nc.scalar.copy(wvo[:], ps_o[:, 0:P]).then_inc(wvo_ready, 1)
            act.wait_ge(decay_loaded, 16)
            sigmoid_qk(0)
            sequence(0)
            with act.Fori(1, B - 1) as b:
                sequence(b)
            sequence(B - 1, last=True)

        @block.vector
        def _(dve):
            def norm_stats(b):
                dve.wait_ge(x_loaded, (b + 1) * 16)
                for n in range(NB):
                    nc.vector.bn_stats(stats[:, n], x_all[:, b * NB + n, :]).then_inc(stats_ready, 1)

            def norm_aggregate(b):
                for n in range(NB):
                    last = nc.vector.bn_aggr(mean_var[:, n], stats[:, n])
                last.then_inc(mean_var_ready, 1)

            def norm_apply(b):
                dve.wait_ge(mean_var_ready, b + 1)
                dve.wait_ge(rstd_ready, b + 1)
                for n in range(NB):
                    nc.vector.tensor_scalar(xn[:, n], x_all[:, b * NB + n, :], mean_var[:, n, 0:1], rstd[:, n:n + 1],
                                            ALU.subtract, ALU.mult).then_inc(xn_ready, 1)

            def subtract_xT(b):
                dve.wait_ge(xT_hi_ready, b + 1)
                nc.vector.tensor_tensor(xT_lo[:], ps_t[:], xT_hi[:].bitcast(F32), ALU.subtract).then_inc(xT_lo_ready, 1)

            def residual(b):
                dve.wait_ge(out_psum_ready, b + 1)
                if not isinstance(b, int) or b > 0:
                    dve.wait_ge(y_stored, b * 16)
                nc.vector.tensor_tensor(y_out[:], ps_t[:].rearrange("p (n e) -> p n e", e=E),
                                        x_all[:, bass.ds(b * NB, NB), :], ALU.add).then_inc(y_ready, 1)

            def hidden(b, c):
                dve.wait_ge(sig_g_ready, b * NH + c + 1)
                nc.vector.scalar_tensor_tensor(silu_g[:, c], gate_bank[c][:], SCALE, sig_g[:, c],
                                               ALU.mult, ALU.mult).then_inc(silu_ready, 1)
                dve.wait_ge(silu_ready, b * NH + c + 1)
                dve.wait_ge(up_psum_ready, b * NH + c + 1)
                nc.vector.scalar_tensor_tensor(h[:, c], up_bank[c][:], SCALE * SCALE, silu_g[:, c],
                                               ALU.mult, ALU.mult).then_inc(h_ready, 1)

            def low_h(b, c):
                dve.wait_ge(h_hi_ready, b * NH + c + 1)
                nc.vector.tensor_tensor(h_lo[:, c], h[:, c], h_hi[:, c].bitcast(F32),
                                        ALU.subtract).then_inc(h_lo_ready[c], 1)

            def sequence(b, left, first=False):
                if first:
                    norm_stats(b + 2)
                    norm_apply(b + 1)
                    hidden(b, 0)
                    dve.wait_ge(stats_ready, (b + 3) * NB)
                    dve.wait_ge(xn_ready, (b + 2) * NB)
                    norm_aggregate(b + 2)
                else:
                    if left >= 1:
                        norm_apply(b + 1)
                    if left >= 2:
                        norm_stats(b + 2)
                        dve.wait_ge(stats_ready, (b + 3) * NB)
                    residual(b - 1)
                    if left >= 2:
                        norm_aggregate(b + 2)
                    hidden(b, 0)
                hidden(b, 1)
                dve.wait_ge(att_psum_ready, b + 1)
                nc.vector.tensor_tensor(att[:], ps_a[:].rearrange("p (n t) -> p n t", t=P), mask,
                                        ALU.mult).then_inc(att_ready, 1)
                low_h(b, 0)
                if left >= 1:
                    subtract_xT(b + 1)
                hidden(b, 2)
                if left == 0:
                    low_h(b, 1)
                low_h(b, 2)

            norm_stats(0)
            dve.wait_ge(stats_ready, NB)
            norm_aggregate(0)
            dve.wait_ge(qk_hi_ready, 1)
            nc.vector.tensor_tensor(qk_lo[:].rearrange("p m e -> p (m e)"), attn_f[:, 0:2 * P],
                                    qk_hi[:].rearrange("p m e -> p (m e)").bitcast(F32), ALU.subtract).then_inc(qk_lo_ready, 1)
            for m in range(3):
                if m == 1:
                    norm_apply(0)
                dve.wait_ge(ffn_hi_ready, m + 1)
                nc.vector.tensor_tensor(ffn_lo[:, m], ffn_int[:, m], ffn_hi[:, m].bitcast(F32),
                                        ALU.subtract).then_inc(ffn_lo_ready, 1)
            subtract_xT(0)
            norm_stats(1)
            dve.wait_ge(lo_total_ready, 1)
            nc.vector.tensor_scalar(has_lo[:], ps_a[0:1, 0:1], 0.0, None, ALU.is_gt).then_inc(has_lo_ready, 1)
            dve.wait_ge(stats_ready, 2 * NB)
            norm_aggregate(1)
            dve.wait_ge(decay_loaded, 16)
            dve.wait_ge(mean_var_ready, 2)
            sequence(0, left=B - 1, first=True)
            with dve.Fori(1, B - 2) as b:
                sequence(b, left=2)
            sequence(B - 2, left=1)
            sequence(B - 1, left=0)
            for i, (cols, bank) in enumerate(zip(column_parts(2), (ps_t, ps_q))):
                blocks = slice(i * NB // 2, (i + 1) * NB // 2)
                dve.wait_ge(out_psum_ready, B + i)
                if i == 0:
                    dve.wait_ge(y_stored, (B - 1) * 16)
                nc.vector.tensor_tensor(y_out[:, blocks], bank[:, cols].rearrange("p (n e) -> p n e", e=E),
                                        x_all[:, (B - 1) * NB + blocks.start:(B - 1) * NB + blocks.stop, :],
                                        ALU.add).then_inc(y_ready, 1)

        @block.tensor
        def _(pe):
            def split_product(bank, w_hi, w_lo, x_hi, x_lo, start=True, stop=True):
                nc.tensor.matmul(bank[:], w_hi, x_lo, start=start, stop=False)
                return high_product(bank, w_hi, w_lo, x_hi, stop)

            def high_product(bank, w_hi, w_lo, x_hi, stop=True):
                if w_lo is not None:
                    nc.tensor.matmul(bank[:], w_lo, x_hi, start=False, stop=False)
                return nc.tensor.matmul(bank[:], w_hi, x_hi, start=False, stop=stop)

            def transpose_xn(b, by_block=False):
                if not by_block:
                    pe.wait_ge(xn_ready, (b + 1) * NB)
                for n in range(NB):
                    if by_block:
                        pe.wait_ge(xn_ready, b * NB + n + 1)
                    last = nc.tensor.transpose(ps_t[:, n * P:(n + 1) * P], xn[:, n], identity[:])
                last.then_inc(xT_psum_ready, 1)

            def transpose_out(b):
                pe.wait_ge(oT_ready, b + 1)
                for n in range(NB):
                    last = nc.tensor.transpose(ps_t[:, n * P:(n + 1) * P], oT[:, n * P:(n + 1) * P], identity[:])
                last.then_inc(out_psum_ready, 1)

            def queries(b):
                pe.wait_ge(xT_hi_ready, b + 1)
                nc.tensor.matmul(ps_q[:], qk_hi[:, 0], xT_hi[:], start=True, stop=False)
                nc.tensor.matmul(ps_q[:], qk_lo[:, 0], xT_hi[:], start=False, stop=False)
                pe.wait_ge(xT_lo_ready, b + 1)
                nc.tensor.matmul(ps_q[:], qk_hi[:, 0], xT_lo[:], start=False, stop=True).then_inc(q_psum_ready, 1)

            def keys(b):
                split_product(ps_k, qk_hi[:, 1], qk_lo[:, 1], xT_hi[:], xT_lo[:]).then_inc(k_psum_ready, 1)

            def sequences(with_lo):
                def weight(m, c):
                    chunk = slice(c * P, (c + 1) * P)
                    return ffn_hi[:, m, chunk], ffn_lo[:, m, chunk] if with_lo else None

                def gate_up(b, c):
                    split_product(gate_bank[c], *weight(0, c), xT_hi[:], xT_lo[:]).then_inc(gate_psum_ready, 1)
                    split_product(up_bank[c], *weight(1, c), xT_hi[:], xT_lo[:]).then_inc(up_psum_ready, 1)

                def down(b, c, stop=False):
                    pe.wait_ge(h_lo_ready[c], b + 1)
                    return split_product(ps_o, *weight(2, c), h_hi[:, c], h_lo[:, c], start=False, stop=stop)

                def sequence(b, first=False, last=False):
                    if first:
                        high_product(ps_g, *weight(0, 0), xT_hi[:]).then_inc(gate_psum_ready, 1)
                        high_product(ps_u, *weight(1, 0), xT_hi[:]).then_inc(up_psum_ready, 1)
                    else:
                        gate_up(b, 0)
                        transpose_out(b - 1)
                    pe.wait_ge(q_ready, b + 1)
                    pe.wait_ge(k_ready, b + 1)
                    gate_up(b, 1)
                    pe.wait_ge(xT_ready, b + 1)
                    for n in range(NB):
                        mm = nc.tensor.matmul(ps_v[:, n * P:(n + 1) * P], xT[:, n * P:(n + 1) * P], wvo[:], start=True, stop=True)
                    mm.then_inc(v_psum_ready, 1)
                    if not first:
                        pe.wait_ge(y_ready, b)
                    for n in range(LB):
                        mm = nc.tensor.transpose(ps_t[:, n * P:(n + 1) * P], kT[:, n * P:(n + 1) * P], identity[:])
                    mm.then_inc(k_tok_psum_ready, 1)
                    for n in range(NB):
                        mm = nc.tensor.matmul(ps_a[:, n * P:(n + 1) * P], kT[:, n * P:(n + 1) * P], qT[:, n * P:(n + 1) * P],
                                              start=True, stop=True)
                    mm.then_inc(att_psum_ready, 1)
                    pe.wait_ge(h_ready, b * NH + 1)
                    gate_up(b, 2)
                    pe.wait_ge(k_tok_ready, b + 1)
                    if not last:
                        transpose_xn(b + 1)
                    pe.wait_ge(v_ready, (b + 1) * NB)
                    for n in range(LB):
                        mm = nc.tensor.matmul(ps_v[:, n * P:(n + 1) * P], k_tok[:, n], v_tok[:, n], start=True, stop=True)
                    mm.then_inc(kv_psum_ready, 1)
                    pe.wait_ge(att_ready, b + 1)
                    for n in range(NB):
                        nc.tensor.matmul(ps_o[:, n * P:(n + 1) * P], v_tok[:, n], att[:, n], start=(n == 0), stop=False)
                    down(b, 0)
                    if not last:
                        queries(b + 1)
                        keys(b + 1)
                        down(b, 1)
                    pe.wait_ge(q_state_ready, b + 1)
                    pe.wait_ge(kv_ready, b + 1)
                    for n in range(LB):
                        if n >= 1:
                            pe.wait_ge(state_ready, b * (LB - 1) + n)
                        nc.tensor.matmul(ps_o[:, (n + 1) * P:(n + 2) * P], kv[:, 0] if n == 0 else state[:, n - 1],
                                         q_state[:, n * P:(n + 1) * P], start=False, stop=False)
                    if last:
                        down(b, 1)
                    down(b, 2, stop=True).then_inc(oT_psum_ready, 1)

                sequence(0, first=True)
                with pe.Fori(1, B - 1) as b:
                    sequence(b)
                sequence(B - 1, last=True)
                for i, bank in enumerate((ps_t, ps_q)):
                    pe.wait_ge(oT_ready, B + i)
                    for n in range(i * NB // 2, (i + 1) * NB // 2):
                        mm = nc.tensor.transpose(bank[:, n * P:(n + 1) * P], oT[:, n * P:(n + 1) * P], identity[:])
                    mm.then_inc(out_psum_ready, 1)

            pe.wait_ge(identity_ready, 1)
            def warm_up(n):
                for _ in range(n):
                    nc.tensor.matmul(ps_v[:, 0:P], identity[:], identity[:], start=True, stop=True)

            warm_up(6)
            pe.wait_ge(attn_w_loaded, 16)
            nc.tensor.matmul(ps_o[:, 0:P], wvT, wo_f, start=True, stop=True).then_inc(wvo_psum_ready, 1)
            warm_up(4)
            transpose_xn(0, by_block=True)
            warm_up(3)
            pe.wait_ge(qk_lo_ready, 1)
            queries(0)
            pe.wait_ge(norm_consts_ready, 1)
            for m in range(3):
                pe.wait_ge(lo_sum_ready, m + 1)
                mm = nc.tensor.matmul(ps_a[0:1, 0:1], lo_sum[:, m:m + 1], ones[:], start=(m == 0), stop=(m == 2))
            mm.then_inc(lo_total_ready, 1)
            keys(0)
            pe.wait_ge(ffn_hi_ready, 2)
            for m, bank in enumerate((ps_g, ps_u)):
                nc.tensor.matmul(bank[:], ffn_hi[:, m, 0:P], xT_lo[:], start=True, stop=False)
            pe.wait_ge(wvo_ready, 1)
            pe.wait_ge(has_lo_ready, 1)
            has = pe.value_load(has_lo[0:1, 0:1], min_val=0, max_val=1)
            with pe.If(has > 0):
                sequences(with_lo=True)
            with pe.Else():
                sequences(with_lo=False)


def kernel(**inputs):
    import concourse.bacc as bacc
    from concourse.bass_utils import run_bass_kernel_spmd

    given = {k: np.asarray(v) for k, v in inputs.items()}
    x = np.ascontiguousarray(given["L0_attn_x"])
    B, T, E = x.shape
    HID = given["L0_ffn_w_gate"].shape[0]
    attn_w = np.concatenate([given["L0_attn_Wq"], given["L0_attn_Wk"], given["L0_attn_Wv"].T, given["L0_attn_Wo"],
                             given["L0_attn_bq"][:, None], given["L0_attn_bk"][:, None]], axis=1)
    down = given["L0_ffn_w_down"].T.reshape(HID // P, P, E).transpose(1, 0, 2).reshape(P, HID)
    ffn_w = np.stack([given["L0_ffn_w_gate"].T, given["L0_ffn_w_up"].T, down], axis=1)
    place = np.arange(T, dtype=np.float64)
    by_block = place.reshape(T // P, P)
    seen = np.arange(P)[:, None] <= np.arange(P)[None, :]
    decay = np.concatenate([np.where(seen[:, None, :], (DECAY ** by_block)[None], 0.0).reshape(P, T),
                            np.broadcast_to(DECAY ** place[P:], (P, T - P)),
                            ((1.0 - DECAY) * DECAY ** -by_block).T], axis=1).astype(np.float32)
    arrays = {"x": x, "attn_w": attn_w, "ffn_w": ffn_w, "decay": decay}

    nc = bacc.Bacc("TRN2", target_bir_lowering=False, num_devices=1)
    args = {k: nc.dram_tensor(f"in_{k}", a.shape, mybir.dt.from_np(a.dtype), kind="ExternalInput").ap() for k, a in arrays.items()}
    y = nc.dram_tensor("out_y", (B, T, E), F32, kind="ExternalOutput").ap()
    build(nc, out=y, **args)
    r = run_bass_kernel_spmd(nc, [{f"in_{k}": np.ascontiguousarray(a) for k, a in arrays.items()}], core_ids=[0])
    return r.results[0]["out_y"]
```
